# Optimizing a Trainium2 kernel written in Bass

```python
import numpy as np
import jax
import jax.numpy as jnp

def _softmax(x, axis=-1):
    return jax.nn.softmax(x, axis=axis)

def _gelu(x):
    return jax.nn.gelu(x, approximate=True)

def _silu(x):
    return jax.nn.silu(x)

def _sigmoid(x):
    return jax.nn.sigmoid(x)

def _layernorm(x, axis=-1, eps=1e-05):
    m = jnp.mean(x, axis=axis, keepdims=True)
    v = jnp.var(x, axis=axis, keepdims=True)
    return (x - m) / jnp.sqrt(v + eps)

def _scatter_add(tgt, idx, src, axis=0):
    return tgt.at[idx].add(src)

def _segment_sum(src, seg, n):
    return jax.ops.segment_sum(src, seg, n)
kernel_name = 'mk_perceiver_d1_seqx_r4_cadeea'

def setup_inputs(seed: int=0):
    np.random.seed(seed)
    _w = jnp.asarray

    def _rec_inputs():
        import jax
        import jax.numpy as jnp
        _rk = jax.random.key(seed)
        x = -0.0003929 + 0.9999 * jax.random.normal(jax.random.fold_in(_rk, 1), (32, 32, 256), jnp.float32)
        _lenS = 32 - jax.random.randint(jax.random.fold_in(_rk, 7), (32,), 0, max(1, 32 // 4) + 1, jnp.int32)
        _lenS2 = 257 - jax.random.randint(jax.random.fold_in(_rk, 8), (32,), 0, max(1, 257 // 4) + 1, jnp.int32)
        _ctx_512P = jax.random.normal(jax.random.fold_in(_rk, 11), (32, 16, 128), jnp.float32)
        _ctx_512c = jax.random.dirichlet(jax.random.fold_in(_rk, 511), 0.3 * jnp.ones((16,), jnp.float32), (32, 257))
        _ctx_512t = jnp.einsum('bsk,bkd->bsd', _ctx_512c, _ctx_512P)
        _ctx_512t = _ctx_512t * jax.lax.rsqrt(jnp.mean(jnp.square(_ctx_512t)) + 1e-12) * 0.953939
        ctx_512 = -1.39393e-06 + 0.999914 * (_ctx_512t + 0.3 * jax.random.normal(jax.random.fold_in(_rk, 611), (32, 257, 128), jnp.float32))
        return (x, ctx_512)
    x, ctx_512 = _rec_inputs()

    def _L0_xattn_setup():
        import jax, jax.numpy as jnp
        import numpy as np
        HEADS = 16
        D_MODEL = 256
        IMG_MODEL = 128
        D_K = D_MODEL // HEADS
        key = jax.random.key(seed)
        ks = jax.random.split(key, 12)
        B, LQ, LKV = (8, 512, 256)
        s_dm = 1.0 / np.sqrt(D_MODEL)
        s_im = 1.0 / np.sqrt(IMG_MODEL)
        return {'q': jax.random.normal(ks[0], (B, LQ, D_MODEL), jnp.float32), 'k': jax.random.normal(ks[1], (B, LKV, IMG_MODEL), jnp.float32), 'v': jax.random.normal(ks[2], (B, LKV, IMG_MODEL), jnp.float32), 'Wq': jax.random.normal(ks[3], (D_MODEL, D_MODEL), jnp.float32) * s_dm, 'bq': jnp.zeros((D_MODEL,), jnp.float32), 'Wk': jax.random.normal(ks[4], (IMG_MODEL, D_MODEL), jnp.float32) * s_im, 'bk': jnp.zeros((D_MODEL,), jnp.float32), 'Wv': jax.random.normal(ks[5], (IMG_MODEL, D_MODEL), jnp.float32) * s_im, 'bv': jnp.zeros((D_MODEL,), jnp.float32), 'Wo': jax.random.normal(ks[6], (D_MODEL, D_MODEL), jnp.float32) * s_dm, 'bo': jnp.zeros((D_MODEL,), jnp.float32)}
    _L0_xattn_all = _L0_xattn_setup()
    _L0_xattn_in = {k: v for k, v in _L0_xattn_all.items() if k in ('Wq', 'bq', 'Wk', 'bk', 'Wv', 'bv', 'Wo', 'bo')}
    del _L0_xattn_all

    def _L0_attn_setup():
        import jax, jax.numpy as jnp
        import numpy as np
        EPS = 0.0001

        def mp_normalize(x, axis):
            red = int(np.prod([x.shape[a] for a in axis])) if isinstance(axis, (list, tuple)) else x.shape[axis]
            w = jnp.sqrt(jnp.sum(jnp.square(x.astype(jnp.float32)), axis=axis, keepdims=True))
            w = EPS + w / np.sqrt(red)
            return x / w.astype(x.dtype)

        def mp_linear(x, w, gain):
            fan_in = w.shape[1]
            wn = mp_normalize(w.astype(jnp.float32), axis=(1,)) * (gain / np.sqrt(fan_in))
            return jnp.einsum('bse,oe->bso', x, wn.astype(x.dtype))

        def attention(query, gain, w_q, w_k, w_v, w_o, num_heads=16, attn_balance=0.5):
            B, S, E = query.shape
            hd = E // num_heads
            res = query
            q = mp_linear(query, w_q, gain).reshape(B, S, num_heads, hd).transpose(0, 2, 1, 3)
            k = mp_linear(query, w_k, gain).reshape(B, S, num_heads, hd).transpose(0, 2, 1, 3)
            v = mp_linear(query, w_v, gain).reshape(B, S, num_heads, hd).transpose(0, 2, 1, 3)
            q = mp_normalize(q, axis=(3,))
            k = mp_normalize(k, axis=(3,))
            scores = jnp.einsum('bnsh,bnsk->bnhk', q, k / np.sqrt(S))
            attn = jax.nn.softmax(scores, axis=3)
            o = jnp.einsum('bnhk,bnsk->bnsh', attn, v)
            o = o.transpose(0, 2, 1, 3).reshape(B, S, E)
            out = mp_linear(o, w_o, gain)
            t = attn_balance
            return (res * (1.0 - t) + out * t) / np.sqrt((1 - t) ** 2 + t ** 2)
        key = jax.random.key(seed)
        ks = jax.random.split(key, 5)
        B, S, E = (4, 1024, 256)
        return {'query': jax.random.normal(ks[0], (B, S, E), dtype=jnp.float32), 'gain': jnp.float32(1.0), 'w_q': jax.random.normal(ks[1], (E, E), dtype=jnp.float32), 'w_k': jax.random.normal(ks[2], (E, E), dtype=jnp.float32), 'w_v': jax.random.normal(ks[3], (E, E), dtype=jnp.float32), 'w_o': jax.random.normal(ks[4], (E, E), dtype=jnp.float32)}
    _L0_attn_all = _L0_attn_setup()
    _L0_attn_in = {k: v for k, v in _L0_attn_all.items() if k in ('gain', 'w_q', 'w_k', 'w_v', 'w_o')}
    del _L0_attn_all

    def _L0_ffn_setup():
        import jax, jax.numpy as jnp
        import numpy as np
        E = 8
        H = 256
        M = 512
        K = 2
        SE = 1
        BSZ, SEQ = (2, 256)
        W_SCALE = 0.02
        key = jax.random.key(seed)
        ks = jax.random.split(key, 9)
        return {'x': jax.random.normal(ks[0], (BSZ, SEQ, H), jnp.float32), 'gate_w': jax.random.normal(ks[1], (E, H), jnp.float32) * W_SCALE, 'beta': jnp.zeros((E,), jnp.float32), 'gate_proj_w': jax.random.normal(ks[2], (E, H, M), jnp.float32) * W_SCALE, 'up_proj_w': jax.random.normal(ks[3], (E, H, M), jnp.float32) * W_SCALE, 'down_proj_w': jax.random.normal(ks[4], (E, M, H), jnp.float32) * W_SCALE, 'shared_gate_w': jax.random.normal(ks[5], (SE, H, M), jnp.float32) * W_SCALE, 'shared_up_w': jax.random.normal(ks[6], (SE, H, M), jnp.float32) * W_SCALE, 'shared_down_w': jax.random.normal(ks[7], (SE, M, H), jnp.float32) * W_SCALE}
    _L0_ffn_all = _L0_ffn_setup()
    _L0_ffn_in = {k: v for k, v in _L0_ffn_all.items() if k in ('gate_w', 'beta', 'gate_proj_w', 'up_proj_w', 'down_proj_w', 'shared_gate_w', 'shared_up_w', 'shared_down_w')}
    del _L0_ffn_all
    return {'x': x, 'ctx_512': ctx_512, 'L0_xattn_Wq': _L0_xattn_in['Wq'], 'L0_xattn_bq': _L0_xattn_in['bq'], 'L0_xattn_Wk': _L0_xattn_in['Wk'], 'L0_xattn_bk': _L0_xattn_in['bk'], 'L0_xattn_Wv': _L0_xattn_in['Wv'], 'L0_xattn_bv': _L0_xattn_in['bv'], 'L0_xattn_Wo': _L0_xattn_in['Wo'], 'L0_xattn_bo': _L0_xattn_in['bo'], 'L0_attn_gain': _L0_attn_in['gain'], 'L0_attn_w_q': _L0_attn_in['w_q'], 'L0_attn_w_k': _L0_attn_in['w_k'], 'L0_attn_w_v': _L0_attn_in['w_v'], 'L0_attn_w_o': _L0_attn_in['w_o'], 'L0_ffn_gate_w': _L0_ffn_in['gate_w'], 'L0_ffn_beta': _L0_ffn_in['beta'], 'L0_ffn_gate_proj_w': _L0_ffn_in['gate_proj_w'], 'L0_ffn_up_proj_w': _L0_ffn_in['up_proj_w'], 'L0_ffn_down_proj_w': _L0_ffn_in['down_proj_w'], 'L0_ffn_shared_gate_w': _L0_ffn_in['shared_gate_w'], 'L0_ffn_shared_up_w': _L0_ffn_in['shared_up_w'], 'L0_ffn_shared_down_w': _L0_ffn_in['shared_down_w']}

def reference(x, ctx_512, L0_xattn_Wq, L0_xattn_bq, L0_xattn_Wk, L0_xattn_bk, L0_xattn_Wv, L0_xattn_bv, L0_xattn_Wo, L0_xattn_bo, L0_attn_gain, L0_attn_w_q, L0_attn_w_k, L0_attn_w_v, L0_attn_w_o, L0_ffn_gate_w, L0_ffn_beta, L0_ffn_gate_proj_w, L0_ffn_up_proj_w, L0_ffn_down_proj_w, L0_ffn_shared_gate_w, L0_ffn_shared_up_w, L0_ffn_shared_down_w):
    import jax
    import jax.numpy as jnp

    def _L0_xattn_ref(q, k, v, Wq, bq, Wk, bk, Wv, bv, Wo, bo):
        import jax, jax.numpy as jnp
        import numpy as np
        HEADS = 16
        D_MODEL = 256
        IMG_MODEL = 128
        D_K = D_MODEL // HEADS
        B, LQ, _ = q.shape
        LKV = k.shape[1]
        qh = (q @ Wq + bq).reshape(B, LQ, HEADS, D_K).transpose(0, 2, 1, 3)
        kh = (k @ Wk + bk).reshape(B, LKV, HEADS, D_K).transpose(0, 2, 1, 3)
        vh = (v @ Wv + bv).reshape(B, LKV, HEADS, D_K).transpose(0, 2, 1, 3)
        scale = 1.0 / np.sqrt(D_K)
        scores = jnp.einsum('bhqd,bhkd->bhqk', qh, kh) * scale
        attn = jax.nn.softmax(scores, axis=-1)
        out = jnp.einsum('bhqk,bhkd->bhqd', attn, vh)
        concat = out.transpose(0, 2, 1, 3).reshape(B, LQ, D_MODEL)
        return concat @ Wo + bo

    def _L0_attn_ref(query, gain, w_q, w_k, w_v, w_o):
        import jax, jax.numpy as jnp
        import numpy as np
        EPS = 0.0001

        def mp_normalize(x, axis):
            red = int(np.prod([x.shape[a] for a in axis])) if isinstance(axis, (list, tuple)) else x.shape[axis]
            w = jnp.sqrt(jnp.sum(jnp.square(x.astype(jnp.float32)), axis=axis, keepdims=True))
            w = EPS + w / np.sqrt(red)
            return x / w.astype(x.dtype)

        def mp_linear(x, w, gain):
            fan_in = w.shape[1]
            wn = mp_normalize(w.astype(jnp.float32), axis=(1,)) * (gain / np.sqrt(fan_in))
            return jnp.einsum('bse,oe->bso', x, wn.astype(x.dtype))

        def attention(query, gain, w_q, w_k, w_v, w_o, num_heads=16, attn_balance=0.5):
            B, S, E = query.shape
            hd = E // num_heads
            res = query
            q = mp_linear(query, w_q, gain).reshape(B, S, num_heads, hd).transpose(0, 2, 1, 3)
            k = mp_linear(query, w_k, gain).reshape(B, S, num_heads, hd).transpose(0, 2, 1, 3)
            v = mp_linear(query, w_v, gain).reshape(B, S, num_heads, hd).transpose(0, 2, 1, 3)
            q = mp_normalize(q, axis=(3,))
            k = mp_normalize(k, axis=(3,))
            scores = jnp.einsum('bnsh,bnsk->bnhk', q, k / np.sqrt(S))
            attn = jax.nn.softmax(scores, axis=3)
            o = jnp.einsum('bnhk,bnsk->bnsh', attn, v)
            o = o.transpose(0, 2, 1, 3).reshape(B, S, E)
            out = mp_linear(o, w_o, gain)
            t = attn_balance
            return (res * (1.0 - t) + out * t) / np.sqrt((1 - t) ** 2 + t ** 2)
        return attention(query, gain, w_q, w_k, w_v, w_o)

    def _L0_ffn_ref(x, gate_w, beta, gate_proj_w, up_proj_w, down_proj_w, shared_gate_w, shared_up_w, shared_down_w):
        import jax, jax.numpy as jnp
        import numpy as np
        E = 8
        H = 256
        M = 512
        K = 2
        SE = 1
        BSZ, SEQ = (2, 256)
        W_SCALE = 0.02
        B0, S0, H0 = x.shape
        xt = x.reshape(-1, H0)
        B = xt.shape[0]
        logits = xt @ gate_w.T
        _, idx = jax.lax.top_k(logits + beta, K)
        probs = jax.nn.sigmoid(jnp.take_along_axis(logits, idx, axis=-1))
        c = jnp.zeros((B, E), xt.dtype).at[jnp.arange(B)[:, None], idx].add(probs)
        g = jnp.einsum('bh,ehm->bem', xt, gate_proj_w)
        u = jnp.einsum('bh,ehm->bem', xt, up_proj_w)
        h = jax.nn.silu(g) * u
        eo = jnp.einsum('bem,emh->beh', h, down_proj_w)
        combined = jnp.einsum('beh,be->bh', eo, c)
        sg = jnp.einsum('bh,ehm->bem', xt, shared_gate_w)
        su = jnp.einsum('bh,ehm->bem', xt, shared_up_w)
        sh = jax.nn.silu(sg) * su
        shared_out = jnp.einsum('bem,emh->beh', sh, shared_down_w).sum(axis=1)
        return (combined + shared_out).reshape(B0, S0, H0)
    x = x + _L0_xattn_ref(_layernorm(x, axis=-1), ctx_512, ctx_512, L0_xattn_Wq, L0_xattn_bq, L0_xattn_Wk, L0_xattn_bk, L0_xattn_Wv, L0_xattn_bv, L0_xattn_Wo, L0_xattn_bo)
    x = x + _L0_attn_ref(_layernorm(x, axis=-1), L0_attn_gain, L0_attn_w_q, L0_attn_w_k, L0_attn_w_v, L0_attn_w_o)
    x = x + _L0_ffn_ref(_layernorm(x, axis=-1), L0_ffn_gate_w, L0_ffn_beta, L0_ffn_gate_proj_w, L0_ffn_up_proj_w, L0_ffn_down_proj_w, L0_ffn_shared_gate_w, L0_ffn_shared_up_w, L0_ffn_shared_down_w)
    return x

_drawn_inputs = setup_inputs


def setup_inputs(seed=0):
    import zlib

    import numpy as np

    out = dict(_drawn_inputs(seed))
    spreads = {'L0_xattn_bq': (0.0, 0.362),
     'L0_xattn_bk': (0.0, 0.8),
     'L0_xattn_bv': (0.0, 0.1),
     'L0_xattn_bo': (0.0, 0.1),
     'L0_ffn_beta': (0.0, 0.8)}
    factors = {'L0_ffn_gate_w': 6.343,
     'L0_ffn_gate_proj_w': 5.345,
     'L0_ffn_up_proj_w': 5.312,
     'L0_ffn_down_proj_w': 5.291,
     'L0_ffn_shared_gate_w': 4.5,
     'L0_ffn_shared_up_w': 4.44,
     'L0_ffn_shared_down_w': 4.461}
    for name, (base, spread) in spreads.items():
        noise = np.random.default_rng([zlib.crc32(name.encode()), seed]).standard_normal(out[name].shape)
        drawn = base * np.exp(spread * noise) if base else spread * noise
        out[name] = jnp.asarray(drawn.astype(out[name].dtype))
    for name, factor in factors.items():
        out[name] = (out[name] * factor).astype(out[name].dtype)
    return out
```

```python
import concourse.bass as bass
from concourse import mybir
from contextlib import ExitStack

F32 = mybir.dt.float32
F32R = mybir.dt.float32r
F16 = mybir.dt.float16
I32 = mybir.dt.int32
U32 = mybir.dt.uint32
ALU = mybir.AluOpType
ACT = mybir.ActivationFunctionType
AX = mybir.AxisListType

B, S, E = 32, 32, 256
LK, C = 257, 128
H, D = 16, 16
NE, M = 8, 512
P = 128
TOK = B * S
NT = TOK // P
SPT = P // S
G = 4
CB = 8
NCH = B // CB
CT = CB * S
LKP = LK + 1
TILES = (2 * TOK + NE * (P - 1)) // P
LN_EPS = 1e-5
MP_EPS = 1e-4
MP_MIX = 0.5 / (0.5 ** 2 + 0.5 ** 2) ** 0.5
ATT_SHIFT = -20.0
VW = S + 1


def perceiver_kernel(nc, a, out, xs_dram, ys_dram):
    ctx = ExitStack()
    with ctx:
        def sb(name, shape, dt=F32, stack=ctx):
            return stack.enter_context(nc.sbuf_tensor(name, shape, dt))

        def sem(name):
            return ctx.enter_context(nc.semaphore(name))

        bank = [ctx.enter_context(nc.psum_tensor(f"bank{i}", [P, 512], F32)) for i in range(8)]

        ident = sb("ident", [P, P])
        ident16 = sb("ident16", [P, P], F16)
        head_mask = sb("head_mask", [P, 8, 16])
        quad_mask = sb("quad_mask", [P, 4])
        tri = sb("tri", [P, P])
        ones = sb("ones", [P, P])
        iota_i = sb("iota_i", [P, 32], I32)
        iota_f = sb("iota_f", [P, 32])
        eps_ln = sb("eps_ln", [P, 1])
        shift_c = sb("shift_c", [P, 1])

        x = sb("x", [P, NT, E])
        xn = sb("xn", [P, NT, E])
        xnT = sb("xnT", [P, 2, TOK])
        acc = sb("acc", [P, NT, E])
        ln_st = sb("ln_st", [P, NT, 6])
        ln_mv = sb("ln_mv", [P, NT, 2])
        ln_rs = sb("ln_rs", [P, NT])

        wq = sb("wq", [P, 2, E])
        wk = sb("wk", [P, E])
        wv = sb("wv", [P, E])
        wo = sb("wo", [P, 2, E])
        bq = sb("bq", [P, 2])
        bk = sb("bk", [P, 2])
        bkm = sb("bkm", [P, 2, 8])
        bv = sb("bv", [P, E])
        bo = sb("bo", [P, E])
        wv_hi = sb("wv_hi", [P, E], F32R)
        wv_lo = sb("wv_lo", [P, E], F32R)
        gain = sb("gain", [P, 1])
        gw = sb("gw", [NE, E])
        gwT = sb("gwT", [P, 2, NE])
        beta = sb("beta", [P, NE])
        w4T = sb("w4T", [P, 2, 4, E])

        sa = ExitStack()
        wkT_hi = sb("wkT_hi", [P, 2, P], F32R, sa)
        wkT_lo = sb("wkT_lo", [P, 2, P], F32R, sa)
        wkm_hi = sb("wkm_hi", [P, H, P], F32R, sa)
        wkm_lo = sb("wkm_lo", [P, H, P], F32R, sa)
        q_f = sb("q_f", [P, 2, CT], F32, sa)
        q_hi = sb("q_hi", [P, 2, CT], F32R, sa)
        q_lo = sb("q_lo", [P, 2, CT], F32R, sa)
        qp_hi = sb("qp_hi", [P, CB, G, 4, S], F32R, sa)
        qp_lo = sb("qp_lo", [P, CB, G, 4, S], F32R, sa)
        cT_hi = [sb(f"cT_hi{i}", [P, LKP], F32R, sa) for i in range(4)]
        cT_lo = [sb(f"cT_lo{i}", [P, LKP], F32R, sa) for i in range(4)]
        cin = [sb(f"cin{i}", [P, 4, 2, C], F32, sa) for i in range(2)]
        crow = [sb(f"crow{i}", [1, 4, C], F32, sa) for i in range(2)]
        prob = [sb(f"prob{i}", [P, G, LK], F32, sa) for i in range(4)]
        p_hi = [sb(f"p_hi{i}", [P, G, 256], F16, sa) for i in range(2)]
        p_lo = [sb(f"p_lo{i}", [P, G, 256], F16, sa) for i in range(2)]
        pT = [sb(f"pT{i}", [P, 2, 2, 512], F16, sa) for i in range(2)]
        v_hi = [sb(f"v_hi{i}", [P, 2, E], F16, sa) for i in range(CB)]
        v_lo = [sb(f"v_lo{i}", [P, 2, E], F16, sa) for i in range(CB)]
        negmax = [sb(f"negmax{i}", [P, G], F32, sa) for i in range(4)]
        kb = sb("kb", [P, CB, G], F32, sa)
        stats = sb("stats", [P, B, 2, G], F32, sa)
        sp_tok = sb("sp_tok", [P, 2, NT, H], F32, sa)
        rsum = sb("rsum", [P, NT, H], F32, sa)
        last_all = sb("last_all", [B, C], F32, sa)
        clT = sb("clT", [P, B], F32, sa)
        clb = sb("clb", [P, B, S], F32, sa)
        vl = [sb(f"vl{i}", [P, E], F32, sa) for i in range(2)]
        ccT = sb("ccT", [P, 2, TOK], F32, sa)
        wraw = sb("wraw", [P, 4, 2, E], F32, sa)
        wsq = ccT[:, :, :].rearrange("p a (b n) -> p (a b) n", n=E)
        wss = sb("wss", [P, 4, 2], F32, sa)
        wsc = sb("wsc", [P, 4, 2], F32, sa)
        sa.close()

        sbk = ExitStack()
        qk = sb("qk", [P, NT, 512], F32, sbk)
        sq = [sb(f"sq{i}", [P, 512], F32, sbk) for i in range(2)]
        ss = sb("ss", [P, NT, 32], F32, sbk)
        rn = sb("rn", [P, NT, 32], F32, sbk)
        kn = [sb(f"kn{i}", [P, E], F32, sbk) for i in range(2)]
        qn = [sb(f"qn{i}", [P, E], F32, sbk) for i in range(2)]
        qb = [sb(f"qb{i}", [P, 2, 4, P], F32, sbk) for i in range(2)]
        vT = sb("vT", [P, 2, B + 2, VW], F32, sbk)
        ex = [sb(f"ex{i}", [P, 4, P], F32, sbk) for i in range(2)]
        bd = [sb(f"bd{i}", [P, 4, P], F32, sbk) for i in range(2)]
        rden = [sb(f"rden{i}", [P, 4], F32, sbk) for i in range(2)]
        oT = sb("oT", [P, 2, TOK], F32, sbk)
        sbk.close()

        sc = ExitStack()
        wdn = sb("wdn", [P, NE, 4, E], F32, sc)
        xrow = [sb(f"xrow{i}", [P, E], F32, sc) for i in range(2)]
        xT = [sb(f"xT{i}", [P, 2, P], F32, sc) for i in range(2)]
        sg = [sb(f"sg{i}", [P, M], F32, sc) for i in range(2)]
        hid = [sb(f"hid{i}", [P, M], F32, sc) for i in range(2)]
        hT = [sb(f"hT{i}", [P, 4, P], F32, sc) for i in range(2)]
        yrow = [sb(f"yrow{i}", [P, E], F32, sc) for i in range(2)]
        yg = [sb(f"yg{i}", [P, 2, E], F32, sc) for i in range(2)]
        lg = sb("lg", [P, NT, NE], F32, sc)
        sel = sb("sel", [P, NT, NE], F32, sc)
        top = sb("top", [P, NT, 8], F32, sc)
        tidx = sb("tidx", [P, NT, 8], U32, sc)
        tix = sb("tix", [P, 2, NT], F32, sc)
        oh = sb("oh", [P, 2, NT, NE], F32, sc)
        both = sb("both", [P, NT, NE], F32, sc)
        tmp = sb("tmp", [P, 2, NT, NE], F32, sc)
        gate = sb("gate", [P, 2, NT], F32, sc)
        before = sb("before", [P, NT + 1, NE], F32, sc)
        cnt = sb("cnt", [P, NT, NE], F32, sc)
        slot = sb("slot", [P, NT, NE], F32, sc)
        cmpk = sb("cmpk", [P, NE, 8], F32, sc)
        ntile = sb("ntile", [P, NE], F32, sc)
        tend = sb("tend", [P, NE + 1], F32, sc)
        cmpj = sb("cmpj", [P, 24, NE], F32, sc)
        te_f = sb("te_f", [P, 24], F32, sc)
        te_i = sb("te_i", [P, 24], I32, sc)
        sl_f = sb("sl_f", [P, 2, NT], F32, sc)
        sl_i = sb("sl_i", [P, 2, NT], I32, sc)
        sb("spacer", [P, 128], F32, sc)
        wgu = sb("wgu", [P, NE, 2, 2, M], F32, sc)
        sgu = sb("sgu", [P, 2, 2, M], F32, sc)
        sdn = sb("sdn", [P, 4, E], F32, sc)
        sc.close()

        def s_(names):
            return [sem(n) for n in names.split()]

        ld_x, ld_w, ld_m, ld_b, ld_s, ld_e, ld_d, zero_row, xs_zero = s_("ld_x ld_w ld_m ld_b ld_s ld_e ld_d zero_row xs_zero")
        ld_c = s_("ld_c0 ld_c1")
        pool_k, pool_c, dve_c, act_c = s_("pool_k pool_c dve_c act_c")
        ln_stat, ln_dev, ln_rows, ln_tr, ln_outA, ln_outV = s_("ln_stat ln_dev ln_rows ln_tr ln_outA ln_outV")
        res_bias = sem("res_bias")
        wkt_ps, wkt_ok, cl_ok, gwt_ok = s_("wkt_ps wkt_ok cl_ok gwt_ok")
        w4_sq, w4_rt, w4_n, w4_ps, w4_ok = s_("w4_sq w4_rt w4_n w4_ps w4_ok")
        Q_ps, q_out, q_his, q_los = s_("Q_ps q_out q_his q_los")
        QP_ps, qp_his, qp_los = s_("QP_ps qp_his qp_los")
        C_ps, c_his, c_los = s_("C_ps c_his c_los")
        V_ps, v_his, v_los = s_("V_ps v_his v_los")
        S_ps, mx, mxb, nmx, KB_ps, kb_out, exps, p_his, p_los, p_last = s_("S_ps mx mxb nmx KB_ps kb_out exps p_his p_los p_last")
        T_ps, t_out, U_ps, u_out = s_("T_ps t_out U_ps u_out")
        VL_ps, vl_out, heads_ok, CC_ps, cc_out, WO_ps, x2_ok = s_("VL_ps vl_out heads_ok CC_ps cc_out WO_ps x2_ok")
        QK_ps, qk_out, sq_ok, ss_ok, rt_ok, VT_ps, vt_out = s_("QK_ps qk_out sq_ok ss_ok rt_ok VT_ps vt_out")
        qkn_ok, qbA, qbP, SB_ps, exb, bd_ok, OB_ps, o_out, W2_ps, x3_ok = s_("qkn_ok qbA qbP SB_ps exb bd_ok OB_ps o_out W2_ps x3_ok")
        LG_ps, both_ok, RK_ps, gl_ok, ge_ok, te_ok, slot_ok, scat = s_("LG_ps both_ok RK_ps gl_ok ge_ok te_ok slot_ok scat")
        row_in, y_st, g_in = s_("row_in0 row_in1"), s_("y_st0 y_st1"), s_("g_in0 g_in1")
        XT_ps, xt_out, GU_ps, silu_ok, hid_ok, HT_ps, ht_out, Y_ps, y_out = s_("XT_ps xt_out GU_ps silu_ok hid_ok HT_ps ht_out Y_ps y_out")
        o_ok, stored = s_("o_ok stored")
        N_SMALL, N_BIAS = 7, 4

        x_rows = a["x"].rearrange("b s e -> (b s) e").rearrange("(t p) e -> p t e", p=P)
        out_rows = out.rearrange("b s e -> (b s) e").rearrange("(t p) e -> p t e", p=P)
        c_rows = a["ctx_512"][:, 0:256, :].rearrange("b (t p) c -> p b t c", p=P)

        ps_s = bank[0:4]
        ps_t = bank[4:6]
        ps_x = bank[6]
        ps_u = bank[7]

        def wait(eng, s, v):
            if not isinstance(v, int) or v > 0:
                eng.wait_ge(s, v)

        def heads(v):
            return v.rearrange("p (h d) -> p h d", d=D)

        with nc.Block() as block:

            @block.sync
            def _(sp):
                sp.dma_start(x[:, 0:4, :], x_rows[:, 0:4, :]).then_inc(ld_x, 16)
                sp.dma_start(x[:, 4:8, :], x_rows[:, 4:8, :]).then_inc(ld_x, 16)
                sp.dma_start(wk[:, :], a["L0_xattn_Wk"]).then_inc(ld_w, 16)
                sp.dma_start(wq[:, :, :], a["L0_xattn_Wq"].rearrange("(k p) n -> p k n", p=P)).then_inc(ld_w, 16)
                sp.dma_start(wv[:, :], a["L0_xattn_Wv"]).then_inc(ld_w, 16)
                for dst, name in ((bq, "bq"), (bk, "bk")):
                    sp.dma_start(dst[:, :], a["L0_xattn_" + name].rearrange("(k p) -> p k", p=P), allow_slow_non_contiguous=True).then_inc(ld_w, 16)

                def context(c, h):
                    b0 = c * CB + 4 * h
                    for t in range(2):
                        sp.dma_start(cin[h][:, :, t, :], c_rows[:, bass.ds(b0, 4), t, :]).then_inc(ld_c[h], 16)
                    sp.dma_start(crow[h][:, :, :], a["ctx_512"][bass.ds(b0, 4), 256:257, :].rearrange("b a c -> a b c")).then_inc(ld_c[h], 16)

                context(0, 0)
                context(0, 1)
                sp.dma_start(last_all[:, :], a["ctx_512"][:, 256, :]).then_inc(ld_m, 16)
                sp.dma_start(gw[:, :], a["L0_ffn_gate_w"]).then_inc(ld_m, 16)
                for n, w in enumerate(("w_q", "w_k", "w_v", "w_o")):
                    sp.dma_start(wraw[:, n, :, :], a["L0_attn_" + w].rearrange("(o p) n -> p o n", p=P)).then_inc(ld_m, 16)
                sp.dma_start(wo[:, :, :], a["L0_xattn_Wo"].rearrange("(k p) n -> p k n", p=P)).then_inc(ld_m, 16)
                with sp.Fori(0, NCH - 1) as i:
                    for h in range(2):
                        sp.wait_ge(C_ps, i * CB + 4 * (h + 1))
                        context(i + 1, h)
                sp.wait_ge(WO_ps, NT)
                sp.dma_start(sgu[:, 0, :, :], a["L0_ffn_shared_gate_w"].rearrange("a (k p) m -> p (a k) m", p=P)).then_inc(ld_s, 16)
                sp.dma_start(sgu[:, 1, :, :], a["L0_ffn_shared_up_w"].rearrange("a (k p) m -> p (a k) m", p=P)).then_inc(ld_s, 16)
                sp.dma_start(sdn[:, :, :], a["L0_ffn_shared_down_w"].rearrange("a (k p) n -> p (a k) n", p=P)).then_inc(ld_s, 16)
                for e in range(NE):
                    sp.dma_start(wgu[:, e, 0, :, :], a["L0_ffn_gate_proj_w"][e].rearrange("(k p) m -> p k m", p=P)).then_inc(ld_e, 16)
                    sp.dma_start(wgu[:, e, 1, :, :], a["L0_ffn_up_proj_w"][e].rearrange("(k p) m -> p k m", p=P)).then_inc(ld_e, 16)
                sp.wait_ge(W2_ps, NT)
                for e in range(NE):
                    sp.dma_start(wdn[:, e, :, :], a["L0_ffn_down_proj_w"][e].rearrange("(k p) n -> p k n", p=P)).then_inc(ld_d, 16)

                def rows_in(n, s):
                    sp.dma_start(xrow[s][:, :], xs_dram[bass.ds(n * P, P), :]).then_inc(row_in[s], 16)

                def rows_out(n, s):
                    sp.wait_ge(y_out, n + 1 + NT)
                    sp.dma_start(ys_dram[bass.ds(n * P, P), :], yrow[s][:, :]).then_inc(y_st[s], 16)

                sp.wait_ge(scat, 16 * 2 * NT)
                rows_in(0, 0)
                rows_in(1, 1)
                with sp.Fori(0, (TILES - 3) // 2) as i:
                    for s in range(2):
                        n = i * 2 + s
                        sp.wait_ge(XT_ps, n + 1)
                        rows_in(n + 2, s)
                        rows_out(n, s)
                n = TILES - 3
                sp.wait_ge(XT_ps, n + 1)
                rows_in(n + 2, 0)
                rows_out(n, 0)
                rows_out(n + 1, 1)
                rows_out(n + 2, 0)
                for t in range(NT):
                    sp.wait_ge(o_ok, t + 1)
                    sp.dma_start(out_rows[:, t, :], acc[:, t, :]).then_inc(stored, 16)
                sp.wait_ge(stored, 16 * NT)

            @block.gpsimd
            def _(pool):
                n = [0]

                def link(ins):
                    n[0] += 1
                    ins.then_inc(pool_c, 1)
                    pool.wait_ge(pool_c, n[0])

                for ap, v in ((ones, 1.0), (ident, 0.0), (tri, 1.0), (quad_mask, 1.0), (eps_ln, LN_EPS), (shift_c, ATT_SHIFT)):
                    link(pool.memset(ap[:, :], v))
                link(pool.memset(head_mask[:, :, :], 1.0))
                link(pool.affine_select(out=ident[:, :], in_=ident[:, :], compare_op=ALU.not_equal, fill=1.0,
                                        base=0, pattern=[[-1, P]], channel_multiplier=1))
                link(pool.affine_select(out=head_mask[:, :, :], in_=head_mask[:, :, :], compare_op=ALU.is_ge, fill=0.0,
                                        base=0, pattern=[[-16, 8], [0, 16]], channel_multiplier=1))
                link(pool.affine_select(out=head_mask[:, :, :], in_=head_mask[:, :, :], compare_op=ALU.is_ge, fill=0.0,
                                        base=15, pattern=[[16, 8], [0, 16]], channel_multiplier=-1))
                link(pool.affine_select(out=quad_mask[:, :], in_=quad_mask[:, :], compare_op=ALU.is_ge, fill=0.0,
                                        base=0, pattern=[[-S, 4]], channel_multiplier=1))
                link(pool.affine_select(out=quad_mask[:, :], in_=quad_mask[:, :], compare_op=ALU.is_ge, fill=0.0,
                                        base=S - 1, pattern=[[S, 4]], channel_multiplier=-1))
                link(pool.affine_select(out=tri[:, :], in_=tri[:, :], compare_op=ALU.is_ge, fill=0.0,
                                        base=-1, pattern=[[1, P]], channel_multiplier=-1))
                pool.iota(iota_i[:, :], pattern=[[1, 32]], base=0, channel_multiplier=0).then_inc(pool_k, 1)
                pool.dma_start(bv[:, :], a["L0_xattn_bv"].partition_broadcast(P)).then_inc(ld_b, 16)
                pool.dma_start(bo[:, :], a["L0_xattn_bo"].partition_broadcast(P)).then_inc(ld_b, 16)
                pool.dma_start(beta[:, :], a["L0_ffn_beta"].partition_broadcast(P)).then_inc(ld_b, 16)
                pool.dma_start(gain[:, :], a["L0_attn_gain"].partition_broadcast(P)).then_inc(ld_b, 16)
                pool.memset(acc[:, 0, :], 0.0).then_inc(zero_row, 1)
                pool.wait_ge(zero_row, 1)
                for j in range(TILES):
                    pool.dma_start(xs_dram[j * P:(j + 1) * P, :], acc[:, 0, :]).then_inc(xs_zero, 16)
                pool.wait_ge(ln_rows, NT)
                pool.wait_ge(ld_b, 16 * N_BIAS)
                for t in range(NT):
                    pool.tensor_tensor(out=x[:, t, :], in0=x[:, t, :], in1=bo[:, :], op=ALU.add).then_inc(res_bias, 1)

                def split(c, j):
                    g = c * CB + j
                    pool.wait_ge(exps, g * G + G)
                    wait(pool, T_ps, (g - 1) * 2)
                    pool.tensor_copy(stats[:, bass.ds(g, 1), 1, :],
                                     prob[j % 4][:, :, 256:257].rearrange("p g a -> p a g")).then_inc(p_last, 1)
                    pool.tensor_scalar(out=p_hi[j % 2][:, :, :], in0=prob[j % 4][:, :, 0:256], scalar1=1.0, scalar2=0.0,
                                       op0=ALU.mult, op1=ALU.add).then_inc(p_his, 1)
                    pool.wait_ge(p_his, g + 1)
                    pool.tensor_tensor(out=p_lo[j % 2][:, :, :], in0=prob[j % 4][:, :, 0:256], in1=p_hi[j % 2][:, :, :],
                                       op=ALU.subtract).then_inc(p_los, 1)

                split(0, 0)
                split(0, 1)
                with pool.Fori(0, NCH - 1) as i:
                    for j in range(2, CB):
                        split(i, j)
                    split(i + 1, 0)
                    split(i + 1, 1)
                for j in range(2, CB):
                    split(NCH - 1, j)

                for t in range(NT):
                    pool.wait_ge(qkn_ok, t + 1)
                    wait(pool, SB_ps, 2 * (t - 1))
                    for b in (2, 3):
                        last = pool.tensor_scalar(out=qb[t % 2][:, :, b, :], in0=qn[t % 2][:, :].rearrange("p (h n) -> p h n", h=2),
                                                  scalar1=quad_mask[:, b:b + 1], scalar2=1.0, op0=ALU.mult, op1=ALU.mult)
                    last.then_inc(qbP, 1)

                pool.wait_ge(slot_ok, 1)
                pool.wait_ge(xs_zero, 16 * TILES)
                for t in range(NT):
                    for r in range(2):
                        pool.indirect_dma_start(xs_dram, bass.IndirectOffsetOnAxis(ap=sl_i[:, r, t:t + 1], axis=0),
                                                xn[:, t, :], None).then_inc(scat, 16)
                pool.wait_ge(y_st[0], 16 * (TILES // 2 + 1))
                pool.wait_ge(y_st[1], 16 * (TILES // 2))
                for t in range(NT):
                    wait(pool, o_ok, t - 1)
                    for r in range(2):
                        pool.indirect_dma_start(yg[t % 2][:, r, :], None, ys_dram,
                                                bass.IndirectOffsetOnAxis(ap=sl_i[:, r, t:t + 1], axis=0)).then_inc(g_in[t % 2], 16)

            @block.scalar
            def _(act):
                def copy(o, i):
                    return act.activation(o, i, ACT.Copy)

                def layer_norm(k, banks):
                    act.wait_ge(ln_stat, k + 1)
                    act.activation(ln_rs[:, :], ln_mv[:, :, 1], ACT.Sqrt, bias=eps_ln[:, 0:1]).then_inc(ln_dev, 1)
                    for h in range(2):
                        act.wait_ge(ln_tr, 4 * k + 2 * h + 1)
                        copy(xnT[:, 0, h * 512:(h + 1) * 512], banks[2 * h][:, :]).then_inc(ln_outA, 1)

                act.wait_ge(pool_k, 1)
                layer_norm(0, bank)

                act.wait_ge(w4_sq, 1)
                act.activation(wsc[:, :, :], wss[:, :, :], ACT.Sqrt).then_inc(w4_rt, 1)
                act.wait_ge(w4_ps, 2)
                for n in range(2):
                    copy(w4T[:, n, 0:2, :], bank[n][:, :].rearrange("p (w o) -> p w o", w=2)).then_inc(w4_ok, 1)
                act.wait_ge(w4_ps, 4)
                for n in range(2):
                    copy(w4T[:, n, 2:4, :], bank[2 + n][:, :].rearrange("p (w o) -> p w o", w=2)).then_inc(w4_ok, 1)

                def q_hi_(c):
                    act.wait_ge(q_out, 2 * c + 2)
                    copy(q_hi[:, :, :], q_f[:, :, :]).then_inc(q_his, 1)

                def c_hi_(c, j):
                    g = c * CB + j
                    act.wait_ge(C_ps, g + 1)
                    wait(act, S_ps, 2 * (g - 3))
                    copy(cT_hi[j % 4][:, 0:LK], ps_x[:, 0:LK]).then_inc(c_his, 1)

                def v_hi_(c, j):
                    g = c * CB + j
                    act.wait_ge(V_ps, g + 1)
                    copy(v_hi[j][:, :, :], ps_x[:, :].rearrange("p (t n) -> p t n", t=2)).then_inc(v_his, 1)

                def qp_view(t, p):
                    g, h0 = p // 2, 2 * (p % 2)
                    return t[:, :, g, h0:h0 + 2, :].rearrange("f b h q -> f h b q")

                def qp_hi_(c, p):
                    act.wait_ge(QP_ps, c * CB + p + 1)
                    if p == 0:
                        wait(act, S_ps, 2 * CB * c)
                    copy(qp_view(qp_hi, p), ps_s[p % 4][:, :].rearrange("f (h b q) -> f h b q", h=2, b=CB)).then_inc(qp_his, 1)

                def exp_(c, j, half):
                    n = c * CB + j
                    act.wait_ge(nmx, 2 * n + half + 1)
                    if half == 0:
                        wait(act, p_los, n - 3)
                        wait(act, p_last, n - 3)
                    for g in (2 * half, 2 * half + 1):
                        act.activation(prob[j % 4][:, g, :], ps_s[g][:, 0:LK], ACT.Exp, bias=negmax[j % 4][:, g:g + 1],
                                       accum_out=stats[:, bass.ds(n, 1), 0, g:g + 1]).then_inc(exps, 1)

                def step(c, j, ahead):
                    if j + 2 < CB:
                        exp_(c, j + 2, 0)
                    if j + 3 < CB:
                        c_hi_(c, j + 3)
                    if j + 2 < CB:
                        exp_(c, j + 2, 1)
                    if j + 3 < CB:
                        v_hi_(c, j + 3)

                def prelude(c):
                    q_hi_(c)
                    c_hi_(c, 0)
                    qp_hi_(c, 0)
                    qp_hi_(c, 1)
                    v_hi_(c, 0)
                    qp_hi_(c, 2)
                    qp_hi_(c, 3)
                    c_hi_(c, 1)
                    qp_hi_(c, 4)
                    v_hi_(c, 1)
                    qp_hi_(c, 5)
                    c_hi_(c, 2)
                    qp_hi_(c, 6)
                    v_hi_(c, 2)
                    qp_hi_(c, 7)
                    exp_(c, 0, 0)
                    exp_(c, 0, 1)
                    exp_(c, 1, 0)
                    exp_(c, 1, 1)
                    step(c, 0, True)
                    step(c, 1, True)

                prelude(0)
                with act.Fori(0, NCH - 1) as i:
                    for j in range(2, CB - 2):
                        step(i, j, True)
                    prelude(i + 1)
                for j in range(2, CB - 2):
                    step(NCH - 1, j, True)

                for n in range(4):
                    act.wait_ge(CC_ps, n + 1)
                    copy(ccT[:, n % 2, (n // 2) * 512:(n // 2 + 1) * 512], bank[4 + n][:, :]).then_inc(cc_out, 1)

                layer_norm(1, bank)

                for t in range(NT):
                    act.wait_ge(QK_ps, t + 1)
                    copy(qk[:, t, :], bank[t % 4][:, :]).then_inc(qk_out, 1)
                    act.wait_ge(qk_out, t + 1)
                    wait(act, ss_ok, t - 1)
                    act.activation(sq[t % 2][:, :], qk[:, t, :], ACT.Square).then_inc(sq_ok, 1)
                for n in range(4):
                    h, m = n // 2, n % 2
                    act.wait_ge(VT_ps, n + 1)
                    copy(vT[:, h, 16 * m:16 * m + 16, 0:S], bank[4 + n][:, :].rearrange("p (b s) -> p b s", b=16)).then_inc(vt_out, 1)
                act.wait_ge(ss_ok, NT)
                act.activation(rn[:, :, :], ss[:, :, :], ACT.Sqrt).then_inc(rt_ok, 1)
                for t in range(NT):
                    act.wait_ge(qkn_ok, t + 1)
                    wait(act, SB_ps, 2 * (t - 1))
                    for b in (0, 1):
                        last = act.activation(qb[t % 2][:, :, b, :], qn[t % 2][:, :].rearrange("p (h n) -> p h n", h=2),
                                              ACT.Copy, scale=quad_mask[:, b:b + 1])
                    last.then_inc(qbA, 1)
                    for h in range(2):
                        u = 2 * t + h
                        act.wait_ge(SB_ps, u + 1)
                        wait(act, bd_ok, u - 1)
                        act.activation(ex[u % 2][:, :, :], bank[u % 4][:, :].rearrange("p (b n) -> p b n", b=4),
                                       ACT.Exp, bias=shift_c[:, 0:1]).then_inc(exb, 1)

                layer_norm(2, bank)
                act.wait_ge(gl_ok, 1)
                act.activation(gate[:, :, :], gate[:, :, :], ACT.Exp, scale=-1.0).then_inc(ge_ok, 1)

                def up(q, s):
                    act.wait_ge(GU_ps, q + 1)
                    wait(act, hid_ok, q - 1)
                    act.activation(sg[s][:, :], bank[2 * s][:, :], ACT.Silu).then_inc(silu_ok, 1)

                def down(q, s):
                    act.wait_ge(HT_ps, q + 1)
                    wait(act, Y_ps, q - 1)
                    copy(hT[s][:, :, :], bank[5][:, :].rearrange("p (k n) -> p k n", k=4)).then_inc(ht_out, 1)

                up(0, 0)
                for q in range(NT):
                    up(q + 1, (q + 1) % 2)
                    down(q, q % 2)
                with act.Fori(0, (TILES - 1) // 2) as i:
                    for s in range(2):
                        q = i * 2 + s + NT
                        up(q + 1, 1 - s)
                        down(q, s)
                down(TILES - 1 + NT, 0)

            @block.vector
            def _(dve):
                n = [0]

                def link(ins):
                    n[0] += 1
                    ins.then_inc(dve_c, 1)
                    dve.wait_ge(dve_c, n[0])

                def tt(o, i0, i1, op):
                    return dve.tensor_tensor(out=o, in0=i0, in1=i1, op=op)

                def layer_norm(k, banks, ready):
                    for t in range(NT):
                        ready(t)
                        last = dve.bn_stats(ln_st[:, t, :], x[:, t, :])
                    link(last)
                    for t in range(NT):
                        last = dve.bn_aggr(ln_mv[:, t, :], ln_st[:, t, :])
                    last.then_inc(ln_stat, 1)
                    dve.wait_ge(ln_dev, k + 1)
                    link(dve.reciprocal(ln_rs[:, :], ln_rs[:, :]))
                    for t in range(NT):
                        dve.tensor_scalar(out=xn[:, t, :], in0=x[:, t, :], scalar1=ln_mv[:, t, 0:1], scalar2=ln_rs[:, t:t + 1],
                                          op0=ALU.subtract, op1=ALU.mult).then_inc(ln_rows, 1)
                    for h in range(2):
                        dve.wait_ge(ln_tr, 4 * k + 2 * h + 2)
                        dve.tensor_copy(xnT[:, 1, h * 512:(h + 1) * 512], banks[2 * h + 1][:, :]).then_inc(ln_outV, 1)

                def x_in(t):
                    if t == 0:
                        dve.wait_ge(ld_x, 32)

                layer_norm(0, bank, x_in)
                dve.wait_ge(pool_k, 1)
                dve.tensor_copy(iota_f[:, :], iota_i[:, :]).then_inc(dve_c, 1)
                link(dve.tensor_copy(ident16[:, :], ident[:, :]))
                n[0] += 1
                dve.wait_ge(dve_c, n[0])
                for i in range(4):
                    dve.memset(cT_hi[i][:, LK:LKP].bitcast(F32), 0.0)
                    last = dve.memset(cT_lo[i][:, LK:LKP].bitcast(F32), 0.0)
                link(last)
                dve.wait_ge(ld_w, 80)
                link(dve.tensor_copy(wv_hi[:, :], wv[:, :]))
                link(tt(wv_lo[:, :], wv[:, :], wv_hi[:, :].bitcast(F32), ALU.subtract))
                dve.wait_ge(wkt_ps, 1)
                wkt = bank[4][:, 0:256].rearrange("p (k f) -> p k f", k=2)
                link(dve.tensor_copy(wkT_hi[:, :, :], wkt))
                link(tt(wkT_lo[:, :, :], wkt, wkT_hi[:, :, :].bitcast(F32), ALU.subtract))
                for k in range(2):
                    for dst, src in ((wkm_hi, wkT_hi), (wkm_lo, wkT_lo)):
                        last = tt(dst[:, 8 * k:8 * k + 8, :], src[:, k:k + 1, :].bitcast(F32).to_broadcast([P, 8, P]),
                                  head_mask[:, :, 0:1].to_broadcast([P, 8, P]), ALU.mult)
                for k in range(2):
                    last = dve.tensor_scalar(out=bkm[:, k, :], in0=head_mask[:, :, 0], scalar1=bk[:, k:k + 1], scalar2=None, op0=ALU.mult)
                last.then_inc(wkt_ok, 1)

                def q_out_(c):
                    dve.wait_ge(Q_ps, c + 1)
                    wait(dve, q_los, c)
                    wait(dve, KB_ps, c)
                    wait(dve, q_his, c)
                    for h in range(2):
                        dve.tensor_scalar(out=q_f[:, h, :], in0=ps_u[:, h * CT:(h + 1) * CT], scalar1=bq[:, h:h + 1],
                                          scalar2=float(D) ** -0.5, op0=ALU.add, op1=ALU.mult).then_inc(q_out, 1)
                    dve.wait_ge(q_his, c + 1)
                    tt(q_lo[:, :, :], q_f[:, :, :], q_hi[:, :, :].bitcast(F32), ALU.subtract).then_inc(q_los, 1)

                def c_lo_(c, j):
                    dve.wait_ge(c_his, c * CB + j + 1)
                    tt(cT_lo[j % 4][:, 0:LK], ps_x[:, 0:LK], cT_hi[j % 4][:, 0:LK].bitcast(F32), ALU.subtract).then_inc(c_los, 1)

                def v_lo_(c, j):
                    dve.wait_ge(v_his, c * CB + j + 1)
                    tt(v_lo[j][:, :, :], ps_x[:, :].rearrange("p (t n) -> p t n", t=2), v_hi[j][:, :, :], ALU.subtract).then_inc(v_los, 1)

                def qp_view(t, p):
                    g, h0 = p // 2, 2 * (p % 2)
                    return t[:, :, g, h0:h0 + 2, :].rearrange("f b h q -> f h b q")

                def qp_lo_(c, p):
                    dve.wait_ge(qp_his, c * CB + p + 1)
                    for h in range(2):
                        last = tt(qp_view(qp_lo, p)[:, h, :, :], ps_s[p % 4][:, h * CT:(h + 1) * CT].rearrange("f (b q) -> f b q", b=CB),
                                  qp_view(qp_hi, p)[:, h, :, :].bitcast(F32), ALU.subtract)
                    last.then_inc(qp_los, 1)

                def kb_out_(c):
                    dve.wait_ge(KB_ps, c + 1)
                    wait(dve, nmx, 2 * CB * c)
                    src = ps_u[:, 0:32].rearrange("p (t g h) -> p t g h", t=2, h=4)
                    dst = kb[:, :, :].rearrange("p (t b) g -> p b t g", b=4)
                    for b in range(4):
                        for h in range(4):
                            last = dve.tensor_copy(dst[32 * h:32 * h + 32, b, :, :], src[32 * b:32 * b + 32, :, :, h])
                    last.then_inc(kb_out, 1)

                def max_(c, j, half):
                    g = c * CB + j
                    dve.wait_ge(S_ps, 2 * g + half + 1)
                    wait(dve, exps, (g - 3) * G)
                    for q in (2 * half, 2 * half + 1):
                        last = dve.tensor_reduce(negmax[j % 4][:, q:q + 1], ps_s[q][:, 0:LK], axis=AX.X, op=ALU.max, negate=True)
                    last.then_inc(mx, 1)
                    dve.wait_ge(mx, 2 * g + half + 1)
                    wait(dve, kb_out, c + 1)
                    h2 = slice(2 * half, 2 * half + 2)
                    tt(negmax[j % 4][:, h2], negmax[j % 4][:, h2], kb[:, j, h2], ALU.subtract).then_inc(mxb, 1)
                    dve.wait_ge(mxb, 2 * g + half + 1)
                    last = tt(negmax[j % 4][:, h2], negmax[j % 4][:, h2], kb[:, j, h2], ALU.add)
                    last.then_inc(nmx, 1)

                def t_out_(c, j, kt):
                    g = c * CB + j
                    dve.wait_ge(T_ps, 2 * g + kt + 1)
                    wait(dve, U_ps, g - 1)
                    dve.tensor_copy(pT[j % 2][:, kt, :, :].rearrange("p s n -> p (s n)").bitcast(U32),
                                    ps_t[kt][:, :].bitcast(U32)).then_inc(t_out, 1)

                def u_out_(c, j):
                    g = c * CB + j
                    dve.wait_ge(U_ps, g + 1)
                    qd = j % 4
                    src = ps_u[:, 0:256].rearrange("p (g h d) -> p g h d", g=G, h=4)
                    dst = acc[:, bass.ds(c * 2 + j // 4, 1), :].rearrange("p t (g h d) -> p (t g) h d", g=G, h=4)
                    for h in range(4):
                        last = dve.tensor_copy(dst[32 * qd:32 * qd + 32, :, h, :], src[32 * h:32 * h + 32, :, h, :])
                    last.then_inc(u_out, 1)

                def step(c, j):
                    if j + 2 < CB:
                        max_(c, j + 2, 0)
                    t_out_(c, j, 0)
                    if j + 2 < CB:
                        max_(c, j + 2, 1)
                    t_out_(c, j, 1)
                    if j + 3 < CB:
                        c_lo_(c, j + 3)
                    u_out_(c, j)
                    if j + 3 < CB:
                        v_lo_(c, j + 3)

                def prelude(c, tail):
                    q_out_(c)
                    c_lo_(c, 0)
                    qp_lo_(c, 0)
                    qp_lo_(c, 1)
                    v_lo_(c, 0)
                    qp_lo_(c, 2)
                    qp_lo_(c, 3)
                    c_lo_(c, 1)
                    qp_lo_(c, 4)
                    v_lo_(c, 1)
                    kb_out_(c)
                    qp_lo_(c, 5)
                    c_lo_(c, 2)
                    qp_lo_(c, 6)
                    v_lo_(c, 2)
                    qp_lo_(c, 7)
                    max_(c, 0, 0)
                    max_(c, 0, 1)
                    if tail:
                        step(c - 1, CB - 2)
                    max_(c, 1, 0)
                    max_(c, 1, 1)
                    if tail:
                        step(c - 1, CB - 1)
                    step(c, 0)
                    step(c, 1)

                dve.wait_ge(ld_m, 16 * N_SMALL)
                dve.wait_ge(ld_b, 16 * N_BIAS)
                dve.wait_ge(xs_zero, 16 * TILES)
                for w in range(4):
                    tt(wsq[:, 2 * w:2 * w + 2, :], wraw[:, w, :, :], wraw[:, w, :, :], ALU.mult).then_inc(dve_c, 1)
                n[0] += 4
                dve.wait_ge(dve_c, n[0])
                dve.tensor_reduce(wss[:, :, :], wsq.rearrange("p (w o) n -> p w o n", o=2), axis=AX.X, op=ALU.add).then_inc(w4_sq, 1)
                dve.wait_ge(w4_rt, 1)
                link(dve.tensor_scalar(out=wsc[:, :, :], in0=wsc[:, :, :], scalar1=E ** -0.5, scalar2=MP_EPS, op0=ALU.mult, op1=ALU.add))
                link(dve.reciprocal(wsc[:, :, :], wsc[:, :, :]))
                link(dve.tensor_scalar(out=wsc[:, :, :], in0=wsc[:, :, :], scalar1=gain[:, 0:1], scalar2=E ** -0.5, op0=ALU.mult, op1=ALU.mult))
                for w in range(4):
                    for o in range(2):
                        dve.tensor_scalar(out=wraw[:, w, o, :], in0=wraw[:, w, o, :], scalar1=wsc[:, w, o:o + 1], scalar2=None,
                                          op0=ALU.mult).then_inc(w4_n, 1)
                dve.wait_ge(wkt_ps, 2)
                dve.tensor_copy(gwT[:, :, :], bank[5][:, 0:16].rearrange("p (k e) -> p k e", k=2)).then_inc(gwt_ok, 1)
                link(dve.tensor_copy(clT[:, :], bank[5][:, 32:64]))
                dve.tensor_copy(clb[:, :, :], clT[:, :].rearrange("p (b a) -> p b a", a=1).to_broadcast([P, B, S])).then_inc(cl_ok, 1)

                prelude(0, False)
                with dve.Fori(0, NCH - 1) as i:
                    for j in range(2, CB - 2):
                        step(i, j)
                    prelude(i + 1, True)
                for j in range(2, CB):
                    step(NCH - 1, j)

                dve.wait_ge(exps, B * G)
                dve.wait_ge(p_last, B)
                dve.wait_ge(u_out, B)
                for qd in range(4):
                    for h in range(4):
                        src = stats[32 * h:32 * h + 32, :, :, :].rearrange("p (t b) w g -> p b w t g", b=4)[:, qd, :, :, :]
                        dst = sp_tok[32 * qd:32 * qd + 32, :, :, :].rearrange("p w t (g h) -> p h w t g", h=4)[:, h, :, :, :]
                        for w in range(2):
                            last = dve.tensor_copy(dst[:, w, :, :], src[:, w, :, :])
                link(last)
                link(dve.reciprocal(rsum[:, :, :], sp_tok[:, 0, :, :]))
                for t in range(NT):
                    dve.wait_ge(VL_ps, t + 1)
                    tt(heads(vl[t % 2][:, :]), heads(bank[t % 4][:, 0:E]),
                       sp_tok[:, 1, t, :].rearrange("p (h a) -> p h a", a=1).to_broadcast([P, H, D]), ALU.mult).then_inc(vl_out, 1)
                    dve.wait_ge(vl_out, t + 1)
                    link(tt(acc[:, t, :], acc[:, t, :], vl[t % 2][:, :], ALU.add))
                    link(tt(heads(acc[:, t, :]), heads(acc[:, t, :]),
                            rsum[:, t, :].rearrange("p (h a) -> p h a", a=1).to_broadcast([P, H, D]), ALU.mult))
                    tt(acc[:, t, :], acc[:, t, :], bv[:, :], ALU.add).then_inc(heads_ok, 1)
                dve.wait_ge(res_bias, NT)

                def x2_(t):
                    dve.wait_ge(WO_ps, t + 1)
                    tt(x[:, t, :], x[:, t, :], bank[t % 4][:, 0:E], ALU.add).then_inc(x2_ok, 1)
                    dve.wait_ge(x2_ok, t + 1)

                layer_norm(1, bank, x2_)

                link(dve.memset(vT[:, :, :, S:VW], 1.0))
                link(dve.memset(vT[:, :, B:B + 2, 0:S], 0.0))
                for t in range(NT):
                    dve.wait_ge(sq_ok, t + 1)
                    dve.tensor_reduce(ss[:, t, :], sq[t % 2][:, :].rearrange("p (h d) -> p h d", d=D), axis=AX.X, op=ALU.add).then_inc(ss_ok, 1)
                dve.wait_ge(rt_ok, 1)
                link(dve.tensor_scalar(out=rn[:, :, :], in0=rn[:, :, :], scalar1=D ** -0.5, scalar2=MP_EPS, op0=ALU.mult, op1=ALU.add))
                link(dve.reciprocal(rn[:, :, :], rn[:, :, :]))
                link(dve.tensor_scalar(out=rn[:, :, H:2 * H], in0=rn[:, :, H:2 * H], scalar1=S ** -0.5, scalar2=None, op0=ALU.mult))

                def norm_(t):
                    wait(dve, qbA, t - 1)
                    wait(dve, qbP, t - 1)
                    wait(dve, SB_ps, 2 * (t - 1))
                    for w, dst in ((0, qn), (1, kn)):
                        last = tt(heads(dst[t % 2][:, :]), heads(qk[:, t, w * E:(w + 1) * E]),
                                  rn[:, t, w * H:(w + 1) * H].rearrange("p (h a) -> p h a", a=1).to_broadcast([P, H, D]), ALU.mult)
                    last.then_inc(qkn_ok, 1)

                def mask_(u):
                    dve.wait_ge(exb, u + 1)
                    wait(dve, OB_ps, u - 1)
                    tt(bd[u % 2][:, :, :], ex[u % 2][:, :, :],
                       head_mask[:, :, :].rearrange("p n (a k) -> p a (n k)", a=1).to_broadcast([P, 4, P]), ALU.mult).then_inc(bd_ok, 1)

                def o_(u):
                    t, h = u // 2, u % 2
                    dve.wait_ge(OB_ps, u + 1)
                    blk = bank[4 + u % 4][:, 0:4 * 3 * VW].rearrange("p (b n) -> p b n", b=4)
                    link(dve.reciprocal(rden[u % 2][:, :], blk[:, :, S]))
                    tt(oT[:, h, t * P:(t + 1) * P].rearrange("p (b s) -> p b s", b=4), blk[:, :, 0:S],
                       rden[u % 2][:, :].rearrange("p (b a) -> p b a", a=1).to_broadcast([P, 4, S]), ALU.mult).then_inc(o_out, 1)

                norm_(0)
                norm_(1)
                for t in range(NT):
                    mask_(2 * t)
                    if t > 0:
                        o_(2 * t - 2)
                    mask_(2 * t + 1)
                    if t > 0:
                        o_(2 * t - 1)
                    if t + 2 < NT:
                        norm_(t + 2)
                o_(2 * NT - 2)
                o_(2 * NT - 1)

                def x3_(t):
                    dve.wait_ge(W2_ps, t + 1)
                    link(tt(xn[:, t, :], xn[:, t, :], bank[t % 4][:, 0:E], ALU.add))
                    dve.scalar_tensor_tensor(out=x[:, t, :], in0=xn[:, t, :], scalar=MP_MIX, in1=x[:, t, :], op0=ALU.mult,
                                             op1=ALU.add).then_inc(x3_ok, 1)
                    dve.wait_ge(x3_ok, t + 1)

                layer_norm(2, bank, x3_)

                dve.wait_ge(LG_ps, 1)
                link(dve.tensor_copy(lg[:, :, :], bank[4][:, 0:NT * NE].rearrange("p (t e) -> p t e", t=NT)))
                link(tt(sel[:, :, :], lg[:, :, :], beta[:, :].rearrange("p (a e) -> p a e", a=1).to_broadcast([P, NT, NE]), ALU.add))
                for t in range(NT):
                    last = dve.max(top[:, t, :], sel[:, t, :])
                link(last)
                for t in range(NT):
                    last = dve.max_index(tidx[:, t, :], top[:, t, :], sel[:, t, :])
                link(last)
                link(dve.tensor_copy(tix[:, :, :], tidx[:, :, 0:2].rearrange("p t r -> p r t")))
                for r in range(2):
                    last = tt(oh[:, r, :, :], iota_f[:, 0:NE].rearrange("p (a e) -> p a e", a=1).to_broadcast([P, NT, NE]),
                              tix[:, r, :].rearrange("p (t a) -> p t a", a=1).to_broadcast([P, NT, NE]), ALU.is_equal)
                link(last)
                tt(both[:, :, :], oh[:, 0, :, :], oh[:, 1, :, :], ALU.add).then_inc(both_ok, 1)
                for r in range(2):
                    last = tt(tmp[:, r, :, :], oh[:, r, :, :], lg[:, :, :], ALU.mult)
                link(last)
                dve.tensor_reduce(gate[:, :, :], tmp[:, :, :, :], axis=AX.X, op=ALU.add).then_inc(gl_ok, 1)
                dve.wait_ge(RK_ps, 1)
                link(dve.tensor_copy(cnt[:, :, :], bank[5][:, 0:64].rearrange("p (t e) -> p t e", t=NT)))
                link(dve.memset(before[:, 0, :], 0.0))
                for t in range(NT):
                    link(tt(before[:, t + 1, :], before[:, t, :], cnt[:, t, :], ALU.add))
                link(dve.tensor_scalar(out=cmpk[:, 0, :], in0=iota_f[:, 0:8], scalar1=float(P), scalar2=None, op0=ALU.mult))
                link(dve.tensor_copy(sel[:, 0, :], cmpk[:, 0, :]))
                link(tt(cmpk[:, :, :], before[:, NT, :].rearrange("p (e a) -> p e a", a=1).to_broadcast([P, NE, 8]),
                        sel[:, 0:1, :].to_broadcast([P, NE, 8]), ALU.is_gt))
                link(dve.tensor_reduce(ntile[:, :], cmpk[:, :, :], axis=AX.X, op=ALU.add))
                link(dve.memset(tend[:, 0:1], 0.0))
                for e in range(NE):
                    link(tt(tend[:, e + 1:e + 2], tend[:, e:e + 1], ntile[:, e:e + 1], ALU.add))
                link(dve.tensor_scalar(out=sel[:, 1, :], in0=tend[:, 0:NE], scalar1=float(P), scalar2=None, op0=ALU.mult))
                link(tt(slot[:, :, :], before[:, 0:NT, :], sel[:, 1:2, :].to_broadcast([P, NT, NE]), ALU.add))
                link(tt(slot[:, :, :], slot[:, :, :], bank[6][:, 0:64].rearrange("p (t e) -> p t e", t=NT), ALU.add))
                for r in range(2):
                    last = tt(tmp[:, r, :, :], oh[:, r, :, :], slot[:, :, :], ALU.mult)
                link(last)
                link(dve.tensor_reduce(sl_f[:, :, :], tmp[:, :, :, :], axis=AX.X, op=ALU.add))
                dve.tensor_copy(sl_i[:, :, :], sl_f[:, :, :]).then_inc(slot_ok, 1)
                link(tt(cmpj[:, :, :], iota_f[:, 0:24].rearrange("p (j a) -> p j a", a=1).to_broadcast([P, 24, NE]),
                        tend[:, 1:NE + 1].rearrange("p (a e) -> p a e", a=1).to_broadcast([P, 24, NE]), ALU.is_ge))
                link(dve.tensor_reduce(te_f[:, :], cmpj[:, :, :], axis=AX.X, op=ALU.add))
                dve.tensor_scalar(out=te_i[:, :], in0=te_f[:, :], scalar1=float(NE - 1), scalar2=None, op0=ALU.min).then_inc(te_ok, 1)
                dve.wait_ge(ge_ok, 1)
                link(dve.tensor_scalar(out=gate[:, :, :], in0=gate[:, :, :], scalar1=1.0, scalar2=None, op0=ALU.add))
                link(dve.reciprocal(gate[:, :, :], gate[:, :, :]))

                def up(q, s):
                    dve.wait_ge(silu_ok, q + 1)
                    wait(dve, HT_ps, q - 1)
                    tt(hid[s][:, :], sg[s][:, :], bank[2 * s + 1][:, :], ALU.mult).then_inc(hid_ok, 1)

                def xt_(k, s):
                    dve.wait_ge(XT_ps, k + 1)
                    dve.tensor_copy(xT[s][:, :, :], bank[4][:, 0:256].rearrange("p (k n) -> p k n", k=2)).then_inc(xt_out, 1)

                def y_(q, s, k):
                    dve.wait_ge(Y_ps, q + 1)
                    wait(dve, y_st[s], k)
                    dve.tensor_copy(yrow[s][:, :], bank[6 + s][:, 0:E]).then_inc(y_out, 1)

                up(0, 0)
                for q in range(NT):
                    if q == NT - 1:
                        xt_(0, 0)
                    up(q + 1, (q + 1) % 2)
                    dve.wait_ge(Y_ps, q + 1)
                    tt(acc[:, q, :], x[:, q, :], bank[6 + q % 2][:, 0:E], ALU.add).then_inc(y_out, 1)
                def routed(i):
                    for s in range(2):
                        q = i * 2 + s + NT
                        xt_(i * 2 + s + 1, 1 - s)
                        up(q + 1, 1 - s)
                        y_(q, s, i * 16)

                routed(0)
                with dve.Fori(1, (TILES - 1) // 2) as i:
                    routed(i)
                y_(TILES - 1 + NT, 0, 16 * ((TILES - 1) // 2))
                for t in range(NT):
                    dve.wait_ge(g_in[t % 2], 32 * (t // 2 + 1))
                    link(dve.scalar_tensor_tensor(out=acc[:, t, :], in0=yg[t % 2][:, 0, :], scalar=gate[:, 0, t:t + 1], in1=acc[:, t, :],
                                                  op0=ALU.mult, op1=ALU.add))
                    dve.scalar_tensor_tensor(out=acc[:, t, :], in0=yg[t % 2][:, 1, :], scalar=gate[:, 1, t:t + 1], in1=acc[:, t, :],
                                             op0=ALU.mult, op1=ALU.add).then_inc(o_ok, 1)

            @block.tensor
            def _(pe):
                def mm(o, l, r, first=True, last=True):
                    return pe.matmul(o, l, r, start=first, stop=last)

                def layer_norm(k, banks):
                    for h in range(2):
                        pe.wait_ge(ln_rows, NT * k + 4 * h + 4)
                        for f in range(2):
                            for t in range(4):
                                last = pe.transpose(banks[2 * h + f][:, t * P:(t + 1) * P], xn[:, 4 * h + t, f * P:(f + 1) * P], ident[:, :])
                            last.then_inc(ln_tr, 1)

                pe.wait_ge(pool_k, 1)
                pe.wait_ge(ld_w, 80)
                for k in range(2):
                    last = pe.transpose(bank[4][:, k * P:(k + 1) * P], wk[:, k * P:(k + 1) * P], ident[:, :])
                last.then_inc(wkt_ps, 1)
                layer_norm(0, bank)
                pe.wait_ge(ld_m, 16 * N_SMALL)
                for k in range(2):
                    pe.transpose(bank[5][:, 8 * k:8 * k + 8], gw[:, k * P:(k + 1) * P], ident[0:NE, 0:NE])
                pe.transpose(bank[5][:, 32:64], last_all[:, :], ident[0:B, 0:B]).then_inc(wkt_ps, 1)
                pe.wait_ge(w4_n, 8)
                pe.wait_ge(ln_outA, 2)
                pe.wait_ge(ln_outV, 2)
                for half in range(2):
                    for k in range(2):
                        for w in range(2):
                            for o in range(2):
                                last = pe.transpose(bank[2 * half + k][:, w * E + o * P:w * E + (o + 1) * P],
                                                    wraw[:, 2 * half + w, o, k * P:(k + 1) * P], ident[:, :])
                        last.then_inc(w4_ps, 1)

                def split3(o, l_hi, l_lo, r_hi, r_lo):
                    mm(o, l_hi, r_hi, True, False)
                    mm(o, l_hi, r_lo, False, False)
                    return mm(o, l_lo, r_hi, False, True)

                def q_(c):
                    wait(pe, u_out, (c - 1) * CB + CB - 2)
                    for h in range(2):
                        for k in range(2):
                            last = mm(ps_u[:, h * CT:(h + 1) * CT], wq[:, k, h * P:(h + 1) * P], xnT[:, k, bass.ds(c * CT, CT)], k == 0, k == 1)
                    last.then_inc(Q_ps, 1)

                def kb_(c):
                    pe.wait_ge(q_out, 2 * c + 2)
                    for t in range(2):
                        for k in range(2):
                            last = mm(ps_u[:, t * H + 8 * k:t * H + 8 * k + 8], q_f[:, k, t * P:(t + 1) * P], bkm[:, k, :])
                    last.then_inc(KB_ps, 1)

                def c_(c, j):
                    if j % 4 == 0:
                        pe.wait_ge(ld_c[j // 4], (c + 1) * 48)
                    wait(pe, v_los, c * CB + j)
                    for t in range(2):
                        pe.transpose(ps_x[:, t * P:(t + 1) * P], cin[j // 4][:, j % 4, t, :], ident[:, :])
                    pe.transpose(ps_x[:, 256:257], crow[j // 4][0:1, j % 4, :], ident[0:1, 0:1]).then_inc(C_ps, 1)

                def v_(c, j):
                    pe.wait_ge(c_his, c * CB + j + 1)
                    pe.wait_ge(c_los, c * CB + j + 1)
                    for t in range(2):
                        k = slice(t * P, (t + 1) * P)
                        last = split3(ps_x[:, t * E:(t + 1) * E], cT_hi[j % 4][:, k], cT_lo[j % 4][:, k], wv_hi[:, :], wv_lo[:, :])
                    last.then_inc(V_ps, 1)

                def qp_(c, p):
                    if p < 4:
                        if p == 0:
                            pe.wait_ge(q_his, c + 1)
                            pe.wait_ge(q_los, c + 1)
                            wait(pe, exps, c * CB * G)
                    else:
                        pe.wait_ge(qp_los, c * CB + p - 3)
                    f = p // 4
                    for e in range(2):
                        h = 2 * p + e
                        last = split3(ps_s[p % 4][:, e * CT:(e + 1) * CT], wkm_hi[:, h, :], wkm_lo[:, h, :], q_hi[:, f, :], q_lo[:, f, :])
                    last.then_inc(QP_ps, 1)

                def s_half(c, j, half):
                    n = c * CB + j
                    for g in (2 * half, 2 * half + 1):
                        if j == 0:
                            pe.wait_ge(qp_his, (c + 1) * CB)
                            pe.wait_ge(qp_los, (c + 1) * CB)
                        else:
                            pe.wait_ge(exps, (n - 1) * G + g + 1)
                        last = split3(ps_s[g][:, 0:LKP], qp_hi[:, j, g, :, :].rearrange("f h q -> f (h q)"),
                                      qp_lo[:, j, g, :, :].rearrange("f h q -> f (h q)"), cT_hi[j % 4][:, :], cT_lo[j % 4][:, :])
                    last.then_inc(S_ps, 1)

                def t_(c, j, kt):
                    n = c * CB + j
                    pe.wait_ge(p_los, n + 1)
                    wait(pe, t_out, 2 * n + kt - 1)
                    dst = ps_t[kt][:, :].bitcast(F16)
                    for s, src in enumerate((p_hi[j % 2], p_lo[j % 2])):
                        for g in range(G):
                            last = pe.transpose(dst[:, s * 512 + g * P:s * 512 + (g + 1) * P], src[:, g, kt * P:(kt + 1) * P], ident16[:, :])
                    last.then_inc(T_ps, 1)

                def u_(c, j):
                    n = c * CB + j
                    pe.wait_ge(t_out, 2 * n + 2)
                    pe.wait_ge(v_los, n + 1)
                    wait(pe, u_out, n)
                    for g in range(G):
                        o = ps_u[:, g * 64:(g + 1) * 64]
                        c64 = slice(g * 64, (g + 1) * 64)
                        m = 0
                        for kt in range(2):
                            for ps, v in ((0, v_hi), (0, v_lo), (1, v_hi)):
                                last = mm(o, pT[j % 2][:, kt, ps, g * P:(g + 1) * P], v[j][:, kt, c64], m == 0, m == 5)
                                m += 1
                    last.then_inc(U_ps, 1)

                def step(c, j):
                    if j + 2 < CB:
                        s_half(c, j + 2, 0)
                    t_(c, j, 0)
                    if j + 2 < CB:
                        s_half(c, j + 2, 1)
                    t_(c, j, 1)
                    if j + 3 < CB:
                        c_(c, j + 3)
                    u_(c, j)
                    if j + 3 < CB:
                        v_(c, j + 3)

                def prelude(c, tail):
                    q_(c)
                    c_(c, 0)
                    kb_(c)
                    qp_(c, 0)
                    qp_(c, 1)
                    v_(c, 0)
                    qp_(c, 2)
                    qp_(c, 3)
                    c_(c, 1)
                    qp_(c, 4)
                    v_(c, 1)
                    qp_(c, 5)
                    c_(c, 2)
                    qp_(c, 6)
                    v_(c, 2)
                    qp_(c, 7)
                    s_half(c, 0, 0)
                    s_half(c, 0, 1)
                    pe.wait_ge(kb_out, c + 1)
                    if tail:
                        step(c - 1, CB - 2)
                    s_half(c, 1, 0)
                    s_half(c, 1, 1)
                    if tail:
                        step(c - 1, CB - 1)
                    step(c, 0)
                    step(c, 1)

                pe.wait_ge(wkt_ok, 1)
                pe.wait_ge(w4_ok, 4)
                prelude(0, False)
                with pe.Fori(0, NCH - 1) as i:
                    for j in range(2, CB - 2):
                        step(i, j)
                    prelude(i + 1, True)
                for j in range(2, CB):
                    step(NCH - 1, j)

                pe.wait_ge(exps, B * G)
                pe.wait_ge(cl_ok, 1)
                for t in range(NT):
                    wait(pe, vl_out, t - 3)
                    mm(bank[t % 4][:, 0:E], clb[:, 4 * t:4 * t + 4, :].rearrange("f b s -> f (b s)"), wv[:, :]).then_inc(VL_ps, 1)
                pe.wait_ge(t_out, 2 * B)
                for half in range(2):
                    pe.wait_ge(heads_ok, 4 * half + 4)
                    for k in range(2):
                        for t in range(4):
                            last = pe.transpose(bank[4 + 2 * half + k][:, t * P:(t + 1) * P], acc[:, 4 * half + t, k * P:(k + 1) * P], ident[:, :])
                        last.then_inc(CC_ps, 1)
                for t in range(NT):
                    pe.wait_ge(cc_out, 2 + 2 * (t // 4))
                    wait(pe, x2_ok, t - 3)
                    for k in range(2):
                        last = mm(bank[t % 4][:, 0:E], ccT[:, k, t * P:(t + 1) * P], wo[:, k, :], k == 0, k == 1)
                    last.then_inc(WO_ps, 1)

                layer_norm(1, bank)

                pe.wait_ge(ln_outA, 4)
                pe.wait_ge(ln_outV, 4)
                for t in range(NT):
                    wait(pe, qk_out, t - 3)
                    for k in range(2):
                        last = mm(bank[t % 4][:, :], xnT[:, k, t * P:(t + 1) * P], w4T[:, k, 0:2, :].rearrange("p w o -> p (w o)"), k == 0, k == 1)
                    last.then_inc(QK_ps, 1)
                for u in range(4):
                    h, m = u // 2, u % 2
                    for k in range(2):
                        last = mm(bank[4 + u][:, :], w4T[:, k, 2, h * P:(h + 1) * P], xnT[:, k, m * 512:(m + 1) * 512], k == 0, k == 1)
                    last.then_inc(VT_ps, 1)

                def ob_(u):
                    t, h = u // 2, u % 2
                    pe.wait_ge(bd_ok, u + 1)
                    wait(pe, o_out, u - 3)
                    for b in range(4):
                        s0 = 4 * t + b
                        last = mm(bank[4 + u % 4][:, b * 3 * VW:(b + 1) * 3 * VW], bd[u % 2][:, b, :],
                                  vT[:, h, s0:s0 + 3, :].rearrange("p b s -> p (b s)"))
                    last.then_inc(OB_ps, 1)

                pe.wait_ge(qk_out, NT)
                pe.wait_ge(vt_out, 4)
                for u in range(2 * NT):
                    t, h = u // 2, u % 2
                    pe.wait_ge(qbA, t + 1)
                    pe.wait_ge(qbP, t + 1)
                    wait(pe, exb, u - 3)
                    mm(bank[u % 4][:, :], kn[t % 2][:, h * P:(h + 1) * P], qb[t % 2][:, h, :, :].rearrange("p b n -> p (b n)")).then_inc(SB_ps, 1)
                    if u >= 2:
                        ob_(u - 2)
                ob_(2 * NT - 2)
                ob_(2 * NT - 1)
                pe.wait_ge(exb, 2 * NT)
                for t in range(NT):
                    pe.wait_ge(o_out, 2 * t + 2)
                    wait(pe, x3_ok, t - 3)
                    for k in range(2):
                        last = mm(bank[t % 4][:, 0:E], oT[:, k, t * P:(t + 1) * P], w4T[:, k, 3, :], k == 0, k == 1)
                    last.then_inc(W2_ps, 1)

                layer_norm(2, bank)

                pe.wait_ge(ln_outA, 6)
                pe.wait_ge(ln_outV, 6)
                pe.wait_ge(gwt_ok, 1)
                for t in range(NT):
                    for k in range(2):
                        last = mm(bank[4][:, t * NE:(t + 1) * NE], xnT[:, k, t * P:(t + 1) * P], gwT[:, k, :], k == 0, k == 1)
                last.then_inc(LG_ps, 1)

                def gu(s, lhs, w, e):
                    for n in range(2):
                        for k in range(2):
                            r = w[:, n, k, :] if e is None else w[:, bass.ds(e, 1), n, k, :].rearrange("p a m -> p (a m)")
                            last = mm(bank[2 * s + n][:, :], lhs(k), r, k == 0, k == 1)
                    last.then_inc(GU_ps, 1)

                def up(q, s, lhs, w, e):
                    wait(pe, hid_ok, q - 1)
                    gu(s, lhs, w, e)

                def down(q, s, w, e):
                    pe.wait_ge(hid_ok, q + 1)
                    wait(pe, ht_out, q)
                    for k in range(4):
                        last = pe.transpose(bank[5][:, k * P:(k + 1) * P], hid[s][:, k * P:(k + 1) * P], ident[:, :])
                    last.then_inc(HT_ps, 1)
                    pe.wait_ge(ht_out, q + 1)
                    wait(pe, y_out, q - 1)
                    for k in range(4):
                        r = w[:, k, :] if e is None else w[:, bass.ds(e, 1), k, :].rearrange("p a m -> p (a m)")
                        last = mm(bank[6 + s][:, 0:E], hT[s][:, k, :], r, k == 0, k == 3)
                    last.then_inc(Y_ps, 1)

                def shared(q):
                    up(q, q % 2, lambda k: xnT[:, k, q * P:(q + 1) * P], sgu, None)

                pe.wait_ge(ld_s, 16 * 3)
                shared(0)
                pe.wait_ge(both_ok, 1)
                mm(bank[5][:, 0:64], ones[:, :], both[:, :, :].rearrange("p t e -> p (t e)"))
                mm(bank[6][:, 0:64], tri[:, :], both[:, :, :].rearrange("p t e -> p (t e)")).then_inc(RK_ps, 1)
                for q in range(NT - 1):
                    shared(q + 1)
                    if q == 0:
                        pe.wait_ge(slot_ok, 1)
                    down(q, q % 2, sdn, None)

                def rows(k_sem, done, s):
                    pe.wait_ge(row_in[s], k_sem)
                    wait(pe, xt_out, done)
                    for k in range(2):
                        last = pe.transpose(bank[4][:, k * P:(k + 1) * P], xrow[s][:, k * P:(k + 1) * P], ident[:, :])
                    last.then_inc(XT_ps, 1)
                    pe.wait_ge(xt_out, done + 1)

                rows(16, 0, 0)
                pe.wait_ge(te_ok, 1)
                pe.wait_ge(ld_e, 16 * 2 * NE)
                e0 = pe.value_load(te_i[0:1, 0:1], min_val=0, max_val=NE - 1)
                up(NT, 0, lambda k: xT[0][:, k, :], wgu, e0)
                down(NT - 1, 1, sdn, None)
                pe.wait_ge(ld_d, 16 * NE)
                with pe.Fori(0, (TILES - 1) // 2) as i:
                    for s in range(2):
                        k = i * 2 + s
                        q = k + NT
                        rows((i + s + 1) * 16, k + 1, 1 - s)
                        e1 = pe.value_load(te_i[0:1, bass.ds(k + 1, 1)], min_val=0, max_val=NE - 1)
                        up(q + 1, 1 - s, (lambda z: lambda k: xT[z][:, k, :])(1 - s), wgu, e1)
                        e = pe.value_load(te_i[0:1, bass.ds(k, 1)], min_val=0, max_val=NE - 1)
                        down(q, s, wdn, e)
                e = pe.value_load(te_i[0:1, TILES - 1:TILES], min_val=0, max_val=NE - 1)
                down(TILES - 1 + NT, 0, wdn, e)


_INS = ['x', 'ctx_512', 'L0_xattn_Wq', 'L0_xattn_bq', 'L0_xattn_Wk', 'L0_xattn_bk', 'L0_xattn_Wv', 'L0_xattn_bv',
        'L0_xattn_Wo', 'L0_xattn_bo', 'L0_attn_gain', 'L0_attn_w_q', 'L0_attn_w_k', 'L0_attn_w_v', 'L0_attn_w_o',
        'L0_ffn_gate_w', 'L0_ffn_beta', 'L0_ffn_gate_proj_w', 'L0_ffn_up_proj_w', 'L0_ffn_down_proj_w',
        'L0_ffn_shared_gate_w', 'L0_ffn_shared_up_w', 'L0_ffn_shared_down_w']


def kernel(**inputs):
    import numpy as _np
    import concourse.bacc as _bacc
    from concourse import mybir as _mybir
    from concourse.bass_utils import run_bass_kernel_spmd as _run

    nc = _bacc.Bacc("TRN2", target_bir_lowering=False, num_devices=1)
    arrays, aps = {}, {}
    for name in _INS:
        v = _np.ascontiguousarray(inputs[name])
        if v.ndim == 0:
            v = v.reshape(1)
        arrays[f"in_{name}"] = v
        aps[name] = nc.dram_tensor(f"in_{name}", v.shape, _mybir.dt.from_np(v.dtype), kind="ExternalInput").ap()
    out = nc.dram_tensor("out_0", (B, S, E), F32, kind="ExternalOutput").ap()
    xs = nc.dram_tensor("routed_rows", [TILES * P, E], F32).ap()
    ys = nc.dram_tensor("expert_rows", [TILES * P, E], F32).ap()
    perceiver_kernel(nc, aps, out, xs, ys)
    r = _run(nc, [arrays], core_ids=[0])
    return r.results[0]["out_0"]
```
